# Optimizing a Trainium2 kernel written in Bass

```python
import numpy as np
import jax
import jax.numpy as jnp

def _softmax(x, axis=-1):
    return jax.nn.softmax(x, axis=axis)

def _gelu(x):
    return jax.nn.gelu(x, approximate=True)

def _silu(x):
    return jax.nn.silu(x)

def _sigmoid(x):
    return jax.nn.sigmoid(x)

def _layernorm(x, axis=-1, eps=1e-05):
    m = jnp.mean(x, axis=axis, keepdims=True)
    v = jnp.var(x, axis=axis, keepdims=True)
    return (x - m) / jnp.sqrt(v + eps)

def _scatter_add(tgt, idx, src, axis=0):
    return tgt.at[idx].add(src)

def _segment_sum(src, seg, n):
    return jax.ops.segment_sum(src, seg, n)
kernel_name = 'mk_dlrm_tower_d1_rec_r8_fece21'

def setup_inputs(seed: int=0):
    np.random.seed(seed)
    _w = jnp.asarray

    def _rec_inputs():
        import jax
        import jax.numpy as jnp
        _tk = jax.random.key(seed)
        dense_ctx = jax.random.normal(jax.random.fold_in(_tk, 190), (512, 16), jnp.float32)
        ids = jnp.stack([jax.random.randint(jax.random.fold_in(_tk, 200 + f), (512,), 0, v, jnp.int32) for f, v in enumerate([1000, 1000, 1000, 125000, 12500, 1000, 1250, 12500, 1000, 12500, 12500, 12500, 1250, 1250, 1250, 1250, 1000, 12500, 1000, 1250, 1000, 1000, 12500, 1250, 1250, 1250, 1000])], axis=1)
        tbl_0 = 0.05 * jax.random.normal(jax.random.fold_in(_tk, 500 + 0), (1000, 128), jnp.float32)
        tbl_1 = 0.05 * jax.random.normal(jax.random.fold_in(_tk, 500 + 1), (1000, 128), jnp.float32)
        tbl_2 = 0.05 * jax.random.normal(jax.random.fold_in(_tk, 500 + 2), (1000, 128), jnp.float32)
        tbl_3 = 0.05 * jax.random.normal(jax.random.fold_in(_tk, 500 + 3), (125000, 128), jnp.float32)
        tbl_4 = 0.05 * jax.random.normal(jax.random.fold_in(_tk, 500 + 4), (12500, 128), jnp.float32)
        tbl_5 = 0.05 * jax.random.normal(jax.random.fold_in(_tk, 500 + 5), (1000, 128), jnp.float32)
        tbl_6 = 0.05 * jax.random.normal(jax.random.fold_in(_tk, 500 + 6), (1250, 128), jnp.float32)
        tbl_7 = 0.05 * jax.random.normal(jax.random.fold_in(_tk, 500 + 7), (12500, 128), jnp.float32)
        tbl_8 = 0.05 * jax.random.normal(jax.random.fold_in(_tk, 500 + 8), (1000, 128), jnp.float32)
        tbl_9 = 0.05 * jax.random.normal(jax.random.fold_in(_tk, 500 + 9), (12500, 128), jnp.float32)
        tbl_10 = 0.05 * jax.random.normal(jax.random.fold_in(_tk, 500 + 10), (12500, 128), jnp.float32)
        tbl_11 = 0.05 * jax.random.normal(jax.random.fold_in(_tk, 500 + 11), (12500, 128), jnp.float32)
        tbl_12 = 0.05 * jax.random.normal(jax.random.fold_in(_tk, 500 + 12), (1250, 128), jnp.float32)
        tbl_13 = 0.05 * jax.random.normal(jax.random.fold_in(_tk, 500 + 13), (1250, 128), jnp.float32)
        tbl_14 = 0.05 * jax.random.normal(jax.random.fold_in(_tk, 500 + 14), (1250, 128), jnp.float32)
        tbl_15 = 0.05 * jax.random.normal(jax.random.fold_in(_tk, 500 + 15), (1250, 128), jnp.float32)
        tbl_16 = 0.05 * jax.random.normal(jax.random.fold_in(_tk, 500 + 16), (1000, 128), jnp.float32)
        tbl_17 = 0.05 * jax.random.normal(jax.random.fold_in(_tk, 500 + 17), (12500, 128), jnp.float32)
        tbl_18 = 0.05 * jax.random.normal(jax.random.fold_in(_tk, 500 + 18), (1000, 128), jnp.float32)
        tbl_19 = 0.05 * jax.random.normal(jax.random.fold_in(_tk, 500 + 19), (1250, 128), jnp.float32)
        tbl_20 = 0.05 * jax.random.normal(jax.random.fold_in(_tk, 500 + 20), (1000, 128), jnp.float32)
        tbl_21 = 0.05 * jax.random.normal(jax.random.fold_in(_tk, 500 + 21), (1000, 128), jnp.float32)
        tbl_22 = 0.05 * jax.random.normal(jax.random.fold_in(_tk, 500 + 22), (12500, 128), jnp.float32)
        tbl_23 = 0.05 * jax.random.normal(jax.random.fold_in(_tk, 500 + 23), (1250, 128), jnp.float32)
        tbl_24 = 0.05 * jax.random.normal(jax.random.fold_in(_tk, 500 + 24), (1250, 128), jnp.float32)
        tbl_25 = 0.05 * jax.random.normal(jax.random.fold_in(_tk, 500 + 25), (1250, 128), jnp.float32)
        tbl_26 = 0.05 * jax.random.normal(jax.random.fold_in(_tk, 500 + 26), (1000, 128), jnp.float32)
        _rk = jax.random.fold_in(_tk, 7)
        W_top1 = 0.0521996 * jax.random.normal(jax.random.fold_in(_tk, 801), (367, 512), jnp.float32)
        W_top2 = 0.0441942 * jax.random.normal(jax.random.fold_in(_tk, 802), (512, 256), jnp.float32)
        W_top3 = 0.0625 * jax.random.normal(jax.random.fold_in(_tk, 803), (256, 1), jnp.float32)
        b_top1 = jnp.zeros((512,), jnp.float32)
        b_top2 = jnp.zeros((256,), jnp.float32)
        return (dense_ctx, ids, tbl_0, tbl_1, tbl_2, tbl_3, tbl_4, tbl_5, tbl_6, tbl_7, tbl_8, tbl_9, tbl_10, tbl_11, tbl_12, tbl_13, tbl_14, tbl_15, tbl_16, tbl_17, tbl_18, tbl_19, tbl_20, tbl_21, tbl_22, tbl_23, tbl_24, tbl_25, tbl_26, W_top1, b_top1, W_top2, b_top2, W_top3)
    dense_ctx, ids, tbl_0, tbl_1, tbl_2, tbl_3, tbl_4, tbl_5, tbl_6, tbl_7, tbl_8, tbl_9, tbl_10, tbl_11, tbl_12, tbl_13, tbl_14, tbl_15, tbl_16, tbl_17, tbl_18, tbl_19, tbl_20, tbl_21, tbl_22, tbl_23, tbl_24, tbl_25, tbl_26, W_top1, b_top1, W_top2, b_top2, W_top3 = _rec_inputs()

    def _L0_rec_setup():
        import jax, jax.numpy as jnp
        import numpy as np
        B, F, D = (2048, 27, 128)
        _TRIL_I, _TRIL_J = np.tril_indices(F, k=-1)
        key = jax.random.key(seed)
        features = jax.random.normal(key, (B, F, D), dtype=jnp.float32)
        return {'features': features}
    _L0_rec_all = _L0_rec_setup()
    _L0_rec_in = {k: v for k, v in _L0_rec_all.items() if k in ()}
    del _L0_rec_all
    return {'dense_ctx': dense_ctx, 'ids': ids, 'tbl_0': tbl_0, 'tbl_1': tbl_1, 'tbl_2': tbl_2, 'tbl_3': tbl_3, 'tbl_4': tbl_4, 'tbl_5': tbl_5, 'tbl_6': tbl_6, 'tbl_7': tbl_7, 'tbl_8': tbl_8, 'tbl_9': tbl_9, 'tbl_10': tbl_10, 'tbl_11': tbl_11, 'tbl_12': tbl_12, 'tbl_13': tbl_13, 'tbl_14': tbl_14, 'tbl_15': tbl_15, 'tbl_16': tbl_16, 'tbl_17': tbl_17, 'tbl_18': tbl_18, 'tbl_19': tbl_19, 'tbl_20': tbl_20, 'tbl_21': tbl_21, 'tbl_22': tbl_22, 'tbl_23': tbl_23, 'tbl_24': tbl_24, 'tbl_25': tbl_25, 'tbl_26': tbl_26, 'W_top1': W_top1, 'b_top1': b_top1, 'W_top2': W_top2, 'b_top2': b_top2, 'W_top3': W_top3}

def reference(dense_ctx, ids, tbl_0, tbl_1, tbl_2, tbl_3, tbl_4, tbl_5, tbl_6, tbl_7, tbl_8, tbl_9, tbl_10, tbl_11, tbl_12, tbl_13, tbl_14, tbl_15, tbl_16, tbl_17, tbl_18, tbl_19, tbl_20, tbl_21, tbl_22, tbl_23, tbl_24, tbl_25, tbl_26, W_top1, b_top1, W_top2, b_top2, W_top3):
    import jax
    import jax.numpy as jnp

    def _L0_rec_ref(features):
        import jax, jax.numpy as jnp
        import numpy as np
        B, F, D = (2048, 27, 128)
        _TRIL_I, _TRIL_J = np.tril_indices(F, k=-1)
        xactions = jnp.einsum('bfd,bgd->bfg', features, features)
        activations = xactions[:, _TRIL_I, _TRIL_J]
        return activations
    e = jnp.stack([tbl_0[ids[:, 0]], tbl_1[ids[:, 1]], tbl_2[ids[:, 2]], tbl_3[ids[:, 3]], tbl_4[ids[:, 4]], tbl_5[ids[:, 5]], tbl_6[ids[:, 6]], tbl_7[ids[:, 7]], tbl_8[ids[:, 8]], tbl_9[ids[:, 9]], tbl_10[ids[:, 10]], tbl_11[ids[:, 11]], tbl_12[ids[:, 12]], tbl_13[ids[:, 13]], tbl_14[ids[:, 14]], tbl_15[ids[:, 15]], tbl_16[ids[:, 16]], tbl_17[ids[:, 17]], tbl_18[ids[:, 18]], tbl_19[ids[:, 19]], tbl_20[ids[:, 20]], tbl_21[ids[:, 21]], tbl_22[ids[:, 22]], tbl_23[ids[:, 23]], tbl_24[ids[:, 24]], tbl_25[ids[:, 25]], tbl_26[ids[:, 26]]], axis=1)
    z = _L0_rec_ref(e)
    z = z.reshape(z.shape[0], -1)
    h = jnp.concatenate([z, dense_ctx], axis=1)
    h = jnp.maximum(h @ W_top1 + b_top1, 0.0)
    h = jnp.maximum(h @ W_top2 + b_top2, 0.0)
    y = h @ W_top3
    return y

_drawn_inputs = setup_inputs


def setup_inputs(seed=0):
    import zlib

    import numpy as np

    out = dict(_drawn_inputs(seed))
    spreads = {'b_top1': (0.0, 0.1), 'b_top2': (0.0, 0.1)}
    factors = {}
    for name, (base, spread) in spreads.items():
        noise = np.random.default_rng([zlib.crc32(name.encode()), seed]).standard_normal(out[name].shape)
        drawn = base * np.exp(spread * noise) if base else spread * noise
        out[name] = jnp.asarray(drawn.astype(out[name].dtype))
    for name, factor in factors.items():
        out[name] = (out[name] * factor).astype(out[name].dtype)
    return out
```

```python
from contextlib import ExitStack

import concourse.bass as bass
from concourse import mybir

F32 = mybir.dt.float32
I32 = mybir.dt.int32
ALU = mybir.AluOpType
ACT = mybir.ActivationFunctionType

P = 128
NF = 27
D = 128
B = 512
TILES = B // P
SLOTS = 32
QUADS = P // 4
ROWS = NF // 2
PAIRS = ROWS * NF
ONEHOT_ROWS = 1000
CHUNKS = 8
TP = ONEHOT_ROWS // CHUNKS
ONEHOT = [0, 1, 2, 5, 8, 16]
GATHERED = [f for f in range(NF) if f not in ONEHOT]
SLOT_FEATURE = GATHERED + ONEHOT
NG, NO = len(GATHERED), len(ONEHOT)
GROUPS = [GATHERED[i:i + 4] for i in range(0, NG, 4)]
EARLY = 3
QB = 4
FILLS = QUADS // (2 * QB)


def fold_order():
    order = []
    for r in range(ROWS):
        for c in range(NF):
            order.append((14 + r, c) if c < 14 + r else (c - 13, r))
    return order


def dlrm_tower(nc, ids_pt, ids_oh, tables, dense_t, w1, b1, w2, b2, w3, out):
    N1, N2 = w1.shape[1], w2.shape[1]
    K1 = w1.shape[0]
    KT = (K1 + P - 1) // P
    KL = K1 - (KT - 1) * P
    ZL = PAIRS - (KT - 1) * P
    M1, M2 = N1 // P, N2 // P

    with ExitStack() as ctx:
        def sb(name, shape, dt=F32):
            return ctx.enter_context(nc.sbuf_tensor(name, shape, dt))

        def ps(name, shape):
            return ctx.enter_context(nc.psum_tensor(name, shape, F32))

        def sem(name):
            return ctx.enter_context(nc.semaphore(name))

        ident = sb("ident", [P, P])
        fold_mask = sb("fold_mask", [P, ROWS, ROWS], I32)
        row_id = sb("row_id", [P, CHUNKS])
        ids_sb = sb("ids_sb", [P, TILES * NF], I32)
        ids_row = sb("ids_row", [P, NO, B], I32)
        rows = sb("rows", [P, TILES, NG, D])
        table = sb("table", [P, NO, CHUNKS, D])
        onehot = sb("onehot", [P, CHUNKS, B])
        emb_t = sb("emb_t", [P, TILES, QUADS, 4, SLOTS])
        dots = sb("dots", [P, NF, QUADS])
        dots_t = sb("dots_t", [P, NF, SLOTS])
        fold = sb("fold", [P, ROWS, NF])
        feat_t = sb("feat_t", [P, KT, B])
        w1_sb = sb("w1_sb", [P, KT, N1])
        w2_sb = sb("w2_sb", [P, M1, N2])
        w3_sb = sb("w3_sb", [P, M2])
        b1_sb = sb("b1_sb", [P, M1])
        b2_sb = sb("b2_sb", [P, M2])
        h1 = sb("h1", [P, M1, P])
        h2 = sb("h2", [P, M2, P])
        y_sb = sb("y_sb", [1, B])

        emb_ps = ps("emb_ps", [P, 2, 512])
        dots_ps = ps("dots_ps", [P, 2, 2, 512])
        layer_ps = [ps("layer_v_ps", [P, 512]), ps("layer_s_ps", [P, 512])]
        fold_ps = layer_ps[0]
        y_ps = layer_ps[0][0:1, 0:P]

        ids_in = sem("ids_in")
        ids_row_in = sem("ids_row_in")
        table_in = [sem(f"table{o}_in") for o in range(NO)]
        weights_in = sem("weights_in")
        rows_in = [[sem(f"rows{t}_{g}_in") for g in range(len(GROUPS))] for t in range(TILES)]
        consts_set = sem("consts_set")
        consts_made = sem("consts_made")
        pads_zeroed = sem("pads_zeroed")
        onehot_made = sem("onehot_made")
        onehot_used = sem("onehot_used")
        emb_filled = sem("emb_filled")
        emb_copied = sem("emb_copied")
        dots_filled = sem("dots_filled")
        dots_copied_v = sem("dots_copied_v")
        dots_copied_s = sem("dots_copied_s")
        dots_turned = sem("dots_turned")
        fold_left = sem("fold_left")
        fold_base = sem("fold_base")
        fold_made = sem("fold_made")
        fold_turned = sem("fold_turned")
        feat_copied = sem("feat_copied")
        h1_summed = sem("h1_summed")
        h1_done_v = sem("h1_done_v")
        h1_done_s = sem("h1_done_s")
        h2_summed = sem("h2_summed")
        h2_done_v = sem("h2_done_v")
        h2_done_s = sem("h2_done_s")
        y_summed = sem("y_summed")
        y_copied = sem("y_copied")
        y_out = sem("y_out")

        def emb_use(t, g):
            return NO + t * len(GROUPS) + g

        def dots_src(j, n):
            return (dots_ps[32 * j:32 * j + 32, n % 2, :, 0:QB * 4 * NF]
                    .rearrange("p k (q j g) -> p k q j g", q=QB, j=4)[:, :, :, j, :])

        def dots_dst(j, fill):
            quads = slice(fill * 2 * QB, (fill + 1) * 2 * QB)
            return dots[32 * j:32 * j + 32, :, quads].rearrange("p g (k q) -> p k q g", k=2)

        block = ctx.enter_context(nc.Block())

        @block.sync
        def _(sp):
            sp.dma_start(ids_sb[:, :], ids_pt).then_inc(ids_in, 16)
            for o in range(0, NO, 2):
                sp.dma_start(table[0:TP, o, :, :],
                             tables[ONEHOT[o]].rearrange("(p c) d -> p c d", c=CHUNKS)).then_inc(table_in[o], 16)
            sp.dma_start(w1_sb[:, 0:KT - 1, :],
                         w1[0:(KT - 1) * P, :].rearrange("(k p) n -> p k n", p=P)).then_inc(weights_in, 16)
            sp.dma_start(w1_sb[0:KL, KT - 1, :], w1[(KT - 1) * P:K1, :]).then_inc(weights_in, 16)
            sp.dma_start(w2_sb[:, :, :], w2.rearrange("(k p) n -> p k n", p=P)).then_inc(weights_in, 16)
            sp.wait_ge(y_copied, TILES)
            sp.dma_start(out.rearrange("b o -> o b"), y_sb[:, :]).then_inc(y_out, 16)
            sp.wait_ge(y_out, 16)

        @block.gpsimd
        def _(pool):
            nc.gpsimd.memset(ident[:, :], 0.0).then_inc(consts_set, 1)
            nc.gpsimd.memset(fold_mask[:, :, :], 1).then_inc(consts_set, 1)
            nc.gpsimd.iota(row_id[:, :], [[1, CHUNKS]], base=0, channel_multiplier=CHUNKS,
                           allow_small_or_imprecise_dtypes=True).then_inc(consts_made, 1)
            pool.wait_ge(consts_set, 2)
            nc.gpsimd.affine_select(out=ident[:, :], in_=ident[:, :], compare_op=ALU.not_equal, fill=1.0,
                                    base=0, pattern=[[-1, P]], channel_multiplier=1).then_inc(consts_made, 1)
            nc.gpsimd.affine_select(out=fold_mask[:, :, :], in_=fold_mask[:, :, :], compare_op=ALU.is_ge, fill=0.0,
                                    base=0, pattern=[[-1, ROWS], [1, ROWS]],
                                    channel_multiplier=0).then_inc(consts_made, 1)
            pool.wait_ge(ids_in, 16)
            for t in range(TILES):
                slot = 0
                for g, group in enumerate(GROUPS):
                    for f in group:
                        at = t * NF + f
                        nc.gpsimd.indirect_dma_start(
                            rows[:, t, slot, :], None, tables[f],
                            bass.IndirectOffsetOnAxis(ap=ids_sb[:, at:at + 1], axis=0)).then_inc(rows_in[t][g], 16)
                        slot += 1

        @block.tensor
        def _(pe):
            def lookup(o):
                use = o
                pe.wait_ge(table_in[o], 16)
                if use >= 2:
                    pe.wait_ge(emb_copied, use - 1)
                for c in range(CHUNKS):
                    pe.wait_ge(onehot_made, o * CHUNKS + c + 1)
                    mm = nc.tensor.matmul(emb_ps[:, use % 2, :], table[0:TP, o, c, :], onehot[0:TP, c, :],
                                          start=(c == 0), stop=(c == CHUNKS - 1))
                    mm.then_inc(onehot_used, 1)

            def turn_rows(t, g):
                use = emb_use(t, g)
                pe.wait_ge(rows_in[t][g], 16 * len(GROUPS[g]))
                pe.wait_ge(emb_copied, use - 1)
                for i in range(len(GROUPS[g])):
                    mm = nc.tensor.transpose(emb_ps[:, use % 2, i * P:(i + 1) * P],
                                             rows[:, t, 4 * g + i, :], ident[:, :])
                mm.then_inc(emb_filled, 1)

            def dot_products(t):
                pe.wait_ge(emb_copied, emb_use(t, len(GROUPS)))
                for fill in range(FILLS):
                    n = t * FILLS + fill
                    if n >= 2:
                        pe.wait_ge(dots_copied_v, n - 1)
                        pe.wait_ge(dots_copied_s, n - 1)
                    for q in range(2 * QB):
                        i = fill * 2 * QB + q
                        at = (q % QB) * 4 * NF
                        mm = nc.tensor.matmul(dots_ps[:, n % 2, q // QB, at:at + 4 * NF],
                                              emb_t[:, t, i, :, :].rearrange("d j s -> d (j s)"),
                                              emb_t[:, t, i, :, 0:NF],
                                              start=True, stop=True)
                    mm.then_inc(dots_filled, 1)

            def dense_layers(t):
                cols = slice(t * P, (t + 1) * P)
                pairs = fold[:, :, :].rearrange("p r c -> p (r c)")
                if t == 0:
                    pe.wait_ge(weights_in, 16 * 7)
                pe.wait_ge(fold_made, t + 1)
                pe.wait_ge(fold_left, t + 1)
                if t >= 1:
                    pe.wait_ge(y_copied, t)
                for k in range(KT):
                    m = min(P, PAIRS - k * P)
                    mm = nc.tensor.transpose(fold_ps[0:m, k * P:(k + 1) * P], pairs[:, k * P:k * P + m],
                                             ident[:, :])
                mm.then_inc(fold_turned, 1)
                pe.wait_ge(feat_copied, 2 * t + 2)
                for half in range(2):
                    for i in range(M1 // 2):
                        n = 2 * i + half
                        for k in range(KT):
                            rows_k = P if k < KT - 1 else KL
                            mm = nc.tensor.matmul(layer_ps[half][:, i * P:(i + 1) * P],
                                                  w1_sb[0:rows_k, k, n * P:(n + 1) * P],
                                                  feat_t[0:rows_k, k, cols], start=(k == 0), stop=(k == KT - 1))
                    mm.then_inc(h1_summed, 1)
                pe.wait_ge(h1_done_v, (t + 1) * M1 // 2)
                pe.wait_ge(h1_done_s, (t + 1) * M1 // 2)
                for n in range(M2):
                    for k in range(M1):
                        mm = nc.tensor.matmul(layer_ps[n][:, 0:P], w2_sb[:, k, n * P:(n + 1) * P],
                                              h1[:, k, :], start=(k == 0), stop=(k == M1 - 1))
                    mm.then_inc(h2_summed, 1)
                pe.wait_ge(h2_done_v, t + 1)
                pe.wait_ge(h2_done_s, t + 1)
                for k in range(M2):
                    mm = nc.tensor.matmul(y_ps, w3_sb[:, k:k + 1], h2[:, k, :],
                                          start=(k == 0), stop=(k == M2 - 1))
                mm.then_inc(y_summed, 1)

            for o in range(NO):
                lookup(o)
            pe.wait_ge(consts_made, 3)
            for t in range(TILES):
                for g in range(EARLY):
                    turn_rows(t, g)
                if t >= 1:
                    dense_layers(t - 1)
                for g in range(EARLY, len(GROUPS)):
                    turn_rows(t, g)
                dot_products(t)
            dense_layers(TILES - 1)

        @block.scalar
        def _(act):
            act.dma_start(ids_row[:, :, :].rearrange("p o b -> p (o b)"),
                          ids_oh.partition_broadcast(P)).then_inc(ids_row_in, 16)
            for o in range(1, NO, 2):
                act.dma_start(table[0:TP, o, :, :],
                              tables[ONEHOT[o]].rearrange("(p c) d -> p c d", c=CHUNKS)).then_inc(table_in[o], 16)
            act.dma_start(feat_t[ZL:KL, KT - 1, :], dense_t).then_inc(weights_in, 16)
            act.dma_start(w3_sb[:, :], w3).then_inc(weights_in, 16)
            act.dma_start(b1_sb[:, :], b1).then_inc(weights_in, 16)
            act.dma_start(b2_sb[:, :], b2).then_inc(weights_in, 16)

            def copy_lookup(o):
                act.wait_ge(onehot_used, (o + 1) * CHUNKS)
                nc.scalar.copy(emb_t[:, :, :, :, NG + o].rearrange("d t i j -> d t j i"),
                               emb_ps[:, o % 2, :].rearrange("d (t j i) -> d t j i", t=TILES, j=4)).then_inc(emb_copied, 1)

            def copy_turned(t, g):
                use, n = emb_use(t, g), len(GROUPS[g])
                act.wait_ge(emb_filled, use - NO + 1)
                nc.scalar.copy(emb_t[:, t, :, :, 4 * g:4 * g + n].rearrange("d i j s -> d s j i"),
                               emb_ps[:, use % 2, 0:n * P].rearrange("d (s j i) -> d s j i", s=n, j=4)
                               ).then_inc(emb_copied, 1)

            def copy_dots(t):
                for fill in range(FILLS):
                    n = t * FILLS + fill
                    act.wait_ge(dots_filled, n + 1)
                    if t >= 1 and fill == 0:
                        act.wait_ge(dots_turned, t)
                    for j in (2, 3):
                        last = nc.scalar.copy(dots_dst(j, fill), dots_src(j, n))
                    last.then_inc(dots_copied_s, 1)

            def dense_layers(t):
                act.wait_ge(dots_turned, t + 1)
                if t >= 1:
                    act.wait_ge(fold_turned, t)
                nc.scalar.copy(fold[:, :, 0:14], dots_t[:, 14:NF, 0:14]).then_inc(fold_left, 1)
                if t == 0:
                    act.wait_ge(weights_in, 16 * 7)
                if t >= 1:
                    act.wait_ge(y_summed, t)
                act.wait_ge(h1_summed, 2 * t + 2)
                for i in range(M1 // 2):
                    n = 2 * i + 1
                    nc.scalar.activation(h1[:, n, :], layer_ps[1][:, i * P:(i + 1) * P], ACT.Relu,
                                         bias=b1_sb[:, n:n + 1]).then_inc(h1_done_s, 1)
                act.wait_ge(h2_summed, t * M2 + 2)
                nc.scalar.activation(h2[:, 1, :], layer_ps[1][:, 0:P], ACT.Relu,
                                     bias=b2_sb[:, 1:2]).then_inc(h2_done_s, 1)
                act.wait_ge(y_summed, t + 1)
                nc.scalar.copy(y_sb[:, t * P:(t + 1) * P], y_ps).then_inc(y_copied, 1)

            act.wait_ge(pads_zeroed, 1)
            for o in range(NO):
                copy_lookup(o)
            for t in range(TILES):
                for g in range(EARLY):
                    copy_turned(t, g)
                if t >= 1:
                    dense_layers(t - 1)
                for g in range(EARLY, len(GROUPS)):
                    copy_turned(t, g)
                copy_dots(t)
            dense_layers(TILES - 1)

        @block.vector
        def _(dve):
            nc.vector.memset(emb_t[:, :, :, :, NF:SLOTS].rearrange("d t i j s -> d (t i j) s"), 0.0).then_inc(pads_zeroed, 1)

            def make_onehot(o):
                for c in range(CHUNKS):
                    if o >= 1:
                        dve.wait_ge(onehot_used, (o - 1) * CHUNKS + c + 1)
                    nc.vector.tensor_scalar(onehot[0:TP, c, :], ids_row[0:TP, o, :], row_id[0:TP, c:c + 1], None,
                                            ALU.is_equal).then_inc(onehot_made, 1)

            def copy_dots(t):
                for fill in range(FILLS):
                    n = t * FILLS + fill
                    dve.wait_ge(dots_filled, n + 1)
                    if t >= 1 and fill == 0:
                        dve.wait_ge(dots_turned, t)
                    for j in (0, 1):
                        last = nc.vector.tensor_copy(dots_dst(j, fill), dots_src(j, n))
                    last.then_inc(dots_copied_v, 1)

            def turn_dots(t):
                dve.wait_ge(dots_copied_v, (t + 1) * FILLS)
                dve.wait_ge(dots_copied_s, (t + 1) * FILLS)
                if t >= 1:
                    dve.wait_ge(fold_left, t)
                    dve.wait_ge(fold_made, t)
                nc.vector.transpose(dots_t[:, :, :].rearrange("p g s -> p (g s)"),
                                    dots[:, :, :].rearrange("p g i -> p (g i)")).then_inc(dots_turned, 1)
                dve.wait_ge(dots_turned, t + 1)
                if t >= 1:
                    dve.wait_ge(fold_turned, t)
                nc.vector.tensor_copy(fold[:, :, 14:NF], dots_t[:, 14:NF, 14:NF]).then_inc(fold_base, 1)
                dve.wait_ge(fold_base, t + 1)
                nc.vector.copy_predicated(fold[:, :, 14:NF], fold_mask[:, :, :],
                                          dots_t[:, 0:ROWS, 1:1 + ROWS]).then_inc(fold_made, 1)

            def dense_layers(t):
                cols = slice(t * P, (t + 1) * P)
                dve.wait_ge(fold_turned, t + 1)
                nc.vector.tensor_copy(feat_t[:, 0:KT - 1, cols],
                                      fold_ps[:, 0:(KT - 1) * P].rearrange("p (k b) -> p k b", b=P)
                                      ).then_inc(feat_copied, 1)
                nc.vector.tensor_copy(feat_t[0:ZL, KT - 1, cols],
                                      fold_ps[0:ZL, (KT - 1) * P:KT * P]).then_inc(feat_copied, 1)
                if t == 0:
                    dve.wait_ge(weights_in, 16 * 7)
                if t >= 1:
                    dve.wait_ge(y_summed, t)
                dve.wait_ge(h1_summed, 2 * t + 1)
                for i in range(M1 // 2):
                    n = 2 * i
                    nc.vector.tensor_scalar(h1[:, n, :], layer_ps[0][:, i * P:(i + 1) * P], b1_sb[:, n:n + 1], 0.0,
                                            ALU.add, ALU.max).then_inc(h1_done_v, 1)
                dve.wait_ge(h2_summed, t * M2 + 1)
                nc.vector.tensor_scalar(h2[:, 0, :], layer_ps[0][:, 0:P], b2_sb[:, 0:1], 0.0,
                                        ALU.add, ALU.max).then_inc(h2_done_v, 1)

            dve.wait_ge(ids_row_in, 16)
            dve.wait_ge(consts_made, 3)
            for o in range(NO):
                make_onehot(o)
            for t in range(TILES):
                copy_dots(t)
                turn_dots(t)
                dense_layers(t)


def kernel(**inputs):
    import numpy as np
    import concourse.bacc as bacc
    from concourse.bass_utils import run_bass_kernel_spmd as run

    nc = bacc.Bacc("TRN2", target_bir_lowering=False, num_devices=1)
    arrays = {}

    def given(name, a):
        a = np.ascontiguousarray(a)
        arrays["in_" + name] = a
        return nc.dram_tensor("in_" + name, a.shape, mybir.dt.from_np(a.dtype), kind="ExternalInput").ap()

    ids = np.asarray(inputs["ids"])
    w1 = np.asarray(inputs["W_top1"])
    pair = []
    for a, b in fold_order():
        hi, lo = max(SLOT_FEATURE[a], SLOT_FEATURE[b]), min(SLOT_FEATURE[a], SLOT_FEATURE[b])
        pair.append(hi * (hi - 1) // 2 + lo)
    order = pair + list(range(PAIRS, w1.shape[0]))
    args = [
        given("ids_pt", ids.reshape(TILES, P, NF).transpose(1, 0, 2).reshape(P, TILES * NF)),
        given("ids_oh", ids.T[ONEHOT].reshape(NO * B)),
        [given(f"tbl_{f}", inputs[f"tbl_{f}"]) for f in range(NF)],
        given("dense_t", np.asarray(inputs["dense_ctx"]).T),
        given("w1", w1[order]),
        given("b1", np.asarray(inputs["b_top1"]).reshape(-1, P).T),
        given("w2", inputs["W_top2"]),
        given("b2", np.asarray(inputs["b_top2"]).reshape(-1, P).T),
        given("w3", np.asarray(inputs["W_top3"]).reshape(-1, P).T),
    ]
    out = nc.dram_tensor("out_y", (B, 1), F32, kind="ExternalOutput").ap()
    dlrm_tower(nc, *args, out)
    r = run(nc, [arrays], core_ids=[0])
    return r.results[0]["out_y"]
```

```python
from contextlib import ExitStack

import concourse.bass as bass
from concourse import mybir

F32 = mybir.dt.float32
F32R = mybir.dt.float32r
I32 = mybir.dt.int32
ALU = mybir.AluOpType
ACT = mybir.ActivationFunctionType

P = 128
NF = 27
D = 128
B = 512
TILES = B // P
SLOTS = 32
QUADS = P // 4
ROWS = NF // 2
PAIRS = ROWS * NF
ONEHOT_ROWS = 1000
CHUNKS = 8
TP = ONEHOT_ROWS // CHUNKS
ONEHOT = [0, 1, 2, 5, 8, 16, 18, 20, 21]
GATHERED = [f for f in range(NF) if f not in ONEHOT]
SLOT_FEATURE = GATHERED + ONEHOT
NG, NO = len(GATHERED), len(ONEHOT)
GROUPS = [GATHERED[i:i + 4] for i in range(0, NG, 4)]
QB = 4
TS = 120
IDS_PARTS = [range(0, 1), range(1, 2), range(2, 4), range(4, NO)]
RAW = 4
ONEHOT_CHUNKS = 12
SPLIT = 2
WARM_START = 10
ROW_TILES = 3
FILLS = QUADS // (2 * QB)


def step_order():
    def turns(t):
        return [("turn", t, g) for g in range(len(GROUPS))] if t < TILES else []

    def layers(t):
        return [(name, t) for name in ("fold", "layer1", "layer2", "layer3")] if t >= 0 else []

    order = []
    first = turns(0)
    for o in range(NO):
        order.append(("lookup", o))
        if o >= NO - 1 - len(GROUPS) and first:
            order.append(first.pop(0))
    order += first
    for t in range(TILES):
        before, beside = layers(t - 1), turns(t + 1)
        for n in range(FILLS):
            order.append(("dots", t, n))
            if n == FILLS - 1:
                order.append(("spread", t))
            if n == 0 and t >= 1:
                order.append(("spread_left", t - 1))
            at_once = len(beside) if n == FILLS - 1 else 2 if t == 0 else 1
            if n < FILLS - 1:
                order += before[n:n + 1] + beside[:at_once]
            else:
                order += beside[:at_once] + before[n:]
            beside = beside[at_once:]
    order.append(("spread_left", TILES - 1))
    return order + layers(TILES - 1)


def fold_order():
    order = []
    for r in range(ROWS):
        for c in range(NF):
            order.append((14 + r, c) if c < 14 + r else (c - 13, r))
    return order


def dlrm_tower(nc, ids_pt, ids_oh, tables, dense_t, w1, b1, w2, b2, w3, out):
    N1, N2 = w1.shape[1], w2.shape[1]
    K1 = w1.shape[0]
    KT = (K1 + P - 1) // P
    KL = K1 - (KT - 1) * P
    ZL = PAIRS - (KT - 1) * P
    M1, M2 = N1 // P, N2 // P

    with ExitStack() as ctx:
        def sb(name, shape, dt=F32):
            return ctx.enter_context(nc.sbuf_tensor(name, shape, dt))

        def ps(name, shape):
            return ctx.enter_context(nc.psum_tensor(name, shape, F32))

        def sem(name):
            return ctx.enter_context(nc.semaphore(name))

        ident = sb("ident", [P, P])
        fold_mask = sb("fold_mask", [P, ROWS, ROWS], I32)
        first_row = sb("first_row", [P, 1])
        ids_sb = sb("ids_sb", [P, TILES * NF], I32)
        ids_row = sb("ids_row", [P, NO, B], I32)
        ids_rel = sb("ids_rel", [P, 2, B])
        rows = sb("rows", [P, ROW_TILES, NG, D])
        table = sb("table", [P, RAW, CHUNKS, D])
        table_hi = sb("table_hi", [P, SPLIT, CHUNKS, D], F32R)
        table_lo = sb("table_lo", [P, SPLIT, CHUNKS, D], F32R)
        onehot = sb("onehot", [P, ONEHOT_CHUNKS, B], F32R)
        emb_t = sb("emb_t", [P, TILES, QUADS, 4, SLOTS])
        dots = sb("dots", [P, NF, QUADS])
        dots_t = sb("dots_t", [P, NF, SLOTS])
        fold = sb("fold", [P, ROWS, NF])
        feat_t = sb("feat_t", [P, KT, B])
        w1_sb = sb("w1_sb", [P, KT, N1])
        w2_sb = sb("w2_sb", [P, M1, N2])
        w3_sb = sb("w3_sb", [P, M2])
        b1_sb = sb("b1_sb", [P, M1])
        b2_sb = sb("b2_sb", [P, M2])
        h1 = sb("h1", [P, M1, P])
        h2 = sb("h2", [P, M2, P])
        y_sb = sb("y_sb", [1, B])

        emb_ps = ps("emb_ps", [P, 2, 512])
        dots_ps = ps("dots_ps", [P, 2, 2, 512])
        layer_ps = [ps("layer_v_ps", [P, 512]), ps("layer_s_ps", [P, 512])]
        fold_v_ps, fold_s_ps = layer_ps[0], layer_ps[1][:, 0:P]
        y_ps = layer_ps[0][0:1, 0:P]

        ids_in = sem("ids_in")
        ids_row_in = [sem(f"ids_row{n}_in") for n in range(len(IDS_PARTS))]
        table_in = [sem(f"table{o}_in") for o in range(NO)]
        ids_shifted = sem("ids_shifted")
        weights_in = sem("weights_in")
        hi_made = sem("hi_made")
        lo_made = sem("lo_made")
        rows_in = [[sem(f"rows{t}_{g}_in") for g in range(len(GROUPS))] for t in range(TILES)]
        consts_set = sem("consts_set")
        consts_made = sem("consts_made")
        pads_zeroed = sem("pads_zeroed")
        onehot_made = sem("onehot_made")
        onehot_used = sem("onehot_used")
        lookup_copied = sem("lookup_copied")
        rows_turned = sem("rows_turned")
        turn_copied = sem("turn_copied")
        dots_filled = sem("dots_filled")
        dots_copied_v = sem("dots_copied_v")
        dots_copied_s = sem("dots_copied_s")
        dots_turned = sem("dots_turned")
        fold_left = sem("fold_left")
        fold_base = sem("fold_base")
        fold_made = sem("fold_made")
        fold_turned = sem("fold_turned")
        feat_copied = sem("feat_copied")
        h1_summed = sem("h1_summed")
        h1_done_v = sem("h1_done_v")
        h1_done_s = sem("h1_done_s")
        h2_summed = sem("h2_summed")
        h2_done_v = sem("h2_done_v")
        h2_done_s = sem("h2_done_s")
        y_summed = sem("y_summed")
        y_copied = sem("y_copied")
        y_out = sem("y_out")

        order = step_order()
        turn_use = {s[1:]: n for n, s in enumerate(s for s in order if s[0] == "turn")}
        def lookup_ps(o):
            return dots_ps[:, o // 2 % 2, o % 2, :]

        def dots_src(j, n):
            return (dots_ps[32 * j:32 * j + 32, n % 2, :, 0:QB * 4 * NF]
                    .rearrange("p k (q j g) -> p k q j g", q=QB, j=4)[:, :, :, j, :])

        def dots_dst(j, fill):
            quads = slice(fill * 2 * QB, (fill + 1) * 2 * QB)
            return dots[32 * j:32 * j + 32, :, quads].rearrange("p g (k q) -> p k q g", k=2)

        block = ctx.enter_context(nc.Block())

        def load_table(sp, o):
            src = tables[ONEHOT[o]].rearrange("(p c) d -> p c d", c=CHUNKS)
            sp.dma_start(table[0:TS, o % RAW, :, :], src[0:TS]).then_inc(table_in[o], 16)
            sp.dma_start(table[TS:TP, o % RAW, :, :], src[TS:TP]).then_inc(table_in[o], 16)

        def load_ids(sp, n):
            part = IDS_PARTS[n]
            sp.dma_start(ids_row[:, part.start:part.stop, :].rearrange("p o b -> p (o b)"),
                         ids_oh[part.start * B:part.stop * B].partition_broadcast(P)).then_inc(ids_row_in[n], 16)

        def load_weights(sp):
            sp.dma_start(w1_sb[:, 0:KT - 1, :],
                         w1[0:(KT - 1) * P, :].rearrange("(k p) n -> p k n", p=P)).then_inc(weights_in, 16)
            sp.dma_start(w1_sb[0:KL, KT - 1, :], w1[(KT - 1) * P:K1, :]).then_inc(weights_in, 16)
            sp.dma_start(w2_sb[:, :, :], w2.rearrange("(k p) n -> p k n", p=P)).then_inc(weights_in, 16)
            sp.dma_start(feat_t[ZL:KL, KT - 1, :], dense_t).then_inc(weights_in, 16)
            sp.dma_start(w3_sb[:, :], w3).then_inc(weights_in, 16)
            sp.dma_start(b1_sb[:, :], b1).then_inc(weights_in, 16)
            sp.dma_start(b2_sb[:, :], b2).then_inc(weights_in, 16)

        @block.sync
        def _(sp):
            sp.dma_start(ids_sb[:, :], ids_pt).then_inc(ids_in, 16)
            load_ids(sp, 0)
            load_table(sp, 0)
            load_ids(sp, 1)
            load_table(sp, 1)
            load_ids(sp, 2)
            load_table(sp, 2)
            load_table(sp, 3)
            load_ids(sp, 3)
            for o in range(RAW, NO):
                sp.wait_ge(lo_made, o - RAW + 1)
                load_table(sp, o)
                if o == RAW + 1:
                    load_weights(sp)
            sp.wait_ge(y_copied, TILES)
            sp.dma_start(out.rearrange("b o -> o b"), y_sb[:, :]).then_inc(y_out, 16)
            sp.wait_ge(y_out, 16)

        @block.gpsimd
        def _(pool):
            nc.gpsimd.memset(ident[:, :], 0.0).then_inc(consts_set, 1)
            nc.gpsimd.memset(fold_mask[:, :, :], 1).then_inc(consts_set, 1)
            nc.gpsimd.iota(first_row[:, :], [[0, 1]], base=0, channel_multiplier=-CHUNKS,
                           allow_small_or_imprecise_dtypes=True).then_inc(consts_made, 1)
            pool.wait_ge(consts_set, 2)
            nc.gpsimd.affine_select(out=ident[:, :], in_=ident[:, :], compare_op=ALU.not_equal, fill=1.0,
                                    base=0, pattern=[[-1, P]], channel_multiplier=1).then_inc(consts_made, 1)
            nc.gpsimd.affine_select(out=fold_mask[:, :, :], in_=fold_mask[:, :, :], compare_op=ALU.is_ge, fill=0.0,
                                    base=0, pattern=[[-1, ROWS], [1, ROWS]],
                                    channel_multiplier=0).then_inc(consts_made, 1)
            pool.wait_ge(ids_in, 16)
            for t in range(TILES):
                if t >= ROW_TILES:
                    pool.wait_ge(rows_turned, turn_use[t - ROW_TILES, len(GROUPS) - 1] + 1)
                slot = 0
                for g, group in enumerate(GROUPS):
                    for f in group:
                        at = t * NF + f
                        nc.gpsimd.indirect_dma_start(
                            rows[:, t % ROW_TILES, slot, :], None, tables[f],
                            bass.IndirectOffsetOnAxis(ap=ids_sb[:, at:at + 1], axis=0)).then_inc(rows_in[t][g], 16)
                        slot += 1

        @block.tensor
        def _(pe):
            def warm_up(count):
                for _ in range(count):
                    nc.tensor.matmul(layer_ps[1][:, 0:P], ident[:, :], ident[:, :], start=True, stop=True)

            def lookup(o):
                if o >= 4:
                    pe.wait_ge(lookup_copied, o - 3)
                bank = lookup_ps(o)
                parts = ([(table_hi, c) for c in range(CHUNKS)] + [(table_lo, c) for c in range(CHUNKS)] if o == 0
                         else [(part, c) for c in range(CHUNKS) for part in (table_hi, table_lo)])
                for n, (part, c) in enumerate(parts):
                    if n == 0:
                        pe.wait_ge(hi_made, o + 1)
                    if part is table_lo and c == 0:
                        pe.wait_ge(lo_made, o + 1)
                    if part is table_hi:
                        pe.wait_ge(onehot_made, o * CHUNKS + c + 1)
                    mm = nc.tensor.matmul(bank, part[0:TP, o % SPLIT, c, :],
                                          onehot[0:TP, (o * CHUNKS + c) % ONEHOT_CHUNKS, :],
                                          start=(n == 0), stop=(n == len(parts) - 1))
                    if part is table_lo:
                        mm.then_inc(onehot_used, 1)

            def turn(t, g):
                n = turn_use[t, g]
                if n >= 2:
                    pe.wait_ge(turn_copied, n - 1)
                bank = emb_ps[:, n % 2, :]
                pe.wait_ge(rows_in[t][g], 16 * len(GROUPS[g]))
                for i in range(len(GROUPS[g])):
                    mm = nc.tensor.transpose(bank[:, i * P:(i + 1) * P],
                                             rows[:, t % ROW_TILES, 4 * g + i, :], ident[:, :])
                mm.then_inc(rows_turned, 1)

            def dots_fill(t, fill):
                n = t * FILLS + fill
                if fill == 0:
                    pe.wait_ge(lookup_copied, NO)
                    pe.wait_ge(turn_copied, turn_use[t, len(GROUPS) - 1] + 1)
                if n >= 2:
                    pe.wait_ge(dots_copied_v, n - 1)
                    pe.wait_ge(dots_copied_s, n - 1)
                for q in range(2 * QB):
                    i = fill * 2 * QB + q
                    at = (q % QB) * 4 * NF
                    mm = nc.tensor.matmul(dots_ps[:, n % 2, q // QB, at:at + 4 * NF],
                                          emb_t[:, t, i, :, :].rearrange("d j s -> d (j s)"),
                                          emb_t[:, t, i, :, 0:NF],
                                          start=True, stop=True)
                mm.then_inc(dots_filled, 1)

            def turn_fold(t):
                pairs = fold[:, :, :].rearrange("p r c -> p (r c)")
                pe.wait_ge(fold_made, t + 1)
                pe.wait_ge(fold_left, t + 1)
                if t >= 1:
                    pe.wait_ge(y_copied, t)
                for k in range(KT):
                    m = min(P, PAIRS - k * P)
                    to = fold_s_ps[0:m, :] if k == KT - 1 else fold_v_ps[0:m, k * P:(k + 1) * P]
                    mm = nc.tensor.transpose(to, pairs[:, k * P:k * P + m], ident[:, :])
                mm.then_inc(fold_turned, 1)

            def layer1(t):
                if t == 0:
                    pe.wait_ge(weights_in, 16 * 7)
                pe.wait_ge(feat_copied, 2 * t + 2)
                for half in range(2):
                    for i in range(M1 // 2):
                        n = 2 * i + half
                        for k in range(KT):
                            rows_k = P if k < KT - 1 else KL
                            mm = nc.tensor.matmul(layer_ps[half][:, i * P:(i + 1) * P],
                                                  w1_sb[0:rows_k, k, n * P:(n + 1) * P],
                                                  feat_t[0:rows_k, k, t * P:(t + 1) * P],
                                                  start=(k == 0), stop=(k == KT - 1))
                    mm.then_inc(h1_summed, 1)

            def layer2(t):
                pe.wait_ge(h1_done_v, (t + 1) * M1 // 2)
                ks = [*range(0, M1, 2), *range(1, M1, 2)]
                for n in range(M2):
                    for k in ks:
                        if n == 0 and k == 1:
                            pe.wait_ge(h1_done_s, (t + 1) * M1 // 2)
                        mm = nc.tensor.matmul(layer_ps[n][:, 0:P], w2_sb[:, k, n * P:(n + 1) * P],
                                              h1[:, k, :], start=(k == ks[0]), stop=(k == ks[-1]))
                    mm.then_inc(h2_summed, 1)

            def layer3(t):
                pe.wait_ge(h2_done_v, t + 1)
                pe.wait_ge(h2_done_s, t + 1)
                for k in range(M2):
                    mm = nc.tensor.matmul(y_ps, w3_sb[:, k:k + 1], h2[:, k, :],
                                          start=(k == 0), stop=(k == M2 - 1))
                mm.then_inc(y_summed, 1)

            pe.wait_ge(consts_made, 3)
            warm_up(WARM_START)
            for step, *at in order:
                if step == "lookup":
                    lookup(*at)
                elif step == "turn":
                    turn(*at)
                elif step == "dots":
                    dots_fill(*at)
                elif step == "fold":
                    turn_fold(*at)
                elif step == "layer1":
                    layer1(*at)
                elif step == "layer2":
                    layer2(*at)
                elif step == "layer3":
                    layer3(*at)

        @block.scalar
        def _(act):
            def split_table(o):
                act.wait_ge(table_in[o], 32)
                if o >= SPLIT:
                    act.wait_ge(onehot_used, (o - SPLIT + 1) * CHUNKS)
                nc.scalar.copy(table_hi[0:TP, o % SPLIT, :, :], table[0:TP, o % RAW, :, :]).then_inc(hi_made, 1)

            def shift_ids(o):
                act.wait_ge(ids_row_in[[o in part for part in IDS_PARTS].index(True)], 16)
                if o == 0:
                    act.wait_ge(consts_made, 3)
                if o >= 2:
                    act.wait_ge(onehot_made, (o - 1) * CHUNKS)
                nc.scalar.activation(ids_rel[0:TP, o % 2, :], ids_row[0:TP, o, :], ACT.Identity,
                                     bias=first_row[0:TP, :]).then_inc(ids_shifted, 1)

            def copy_lookup(o):
                act.wait_ge(onehot_used, (o + 1) * CHUNKS)
                if o == 0:
                    act.wait_ge(pads_zeroed, 1)
                nc.scalar.copy(emb_t[:, :, :, :, NG + o].rearrange("d t i j -> d t j i"),
                               lookup_ps(o).rearrange("d (t j i) -> d t j i", t=TILES, j=4)
                               ).then_inc(lookup_copied, 1)

            def copy_turned(t, g):
                use, n = turn_use[t, g], len(GROUPS[g])
                act.wait_ge(rows_turned, use + 1)
                nc.scalar.copy(emb_t[:, t, :, :, 4 * g:4 * g + n].rearrange("d i j s -> d s j i"),
                               emb_ps[:, use % 2, 0:n * P].rearrange("d (s j i) -> d s j i", s=n, j=4)
                               ).then_inc(turn_copied, 1)

            def copy_dots(t, fill):
                n = t * FILLS + fill
                act.wait_ge(dots_filled, n + 1)
                if t >= 1 and fill == 0:
                    act.wait_ge(dots_turned, t)
                for j in (2, 3):
                    last = nc.scalar.copy(dots_dst(j, fill), dots_src(j, n))
                last.then_inc(dots_copied_s, 1)

            def spread_left(t):
                act.wait_ge(dots_turned, t + 1)
                if t >= 1:
                    act.wait_ge(fold_turned, t)
                nc.scalar.copy(fold[:, :, 0:14], dots_t[:, 14:NF, 0:14]).then_inc(fold_left, 1)

            def copy_fold(t):
                act.wait_ge(fold_turned, t + 1)
                nc.scalar.copy(feat_t[0:ZL, KT - 1, t * P:(t + 1) * P], fold_s_ps[0:ZL, :]).then_inc(feat_copied, 1)

            def layer1(t):
                if t == 0:
                    act.wait_ge(weights_in, 16 * 7)
                else:
                    act.wait_ge(y_summed, t)
                act.wait_ge(h1_summed, 2 * t + 2)
                for i in range(M1 // 2):
                    n = 2 * i + 1
                    nc.scalar.activation(h1[:, n, :], layer_ps[1][:, i * P:(i + 1) * P], ACT.Relu,
                                         bias=b1_sb[:, n:n + 1]).then_inc(h1_done_s, 1)

            def layer2(t):
                act.wait_ge(h2_summed, t * M2 + 2)
                nc.scalar.activation(h2[:, 1, :], layer_ps[1][:, 0:P], ACT.Relu,
                                     bias=b2_sb[:, 1:2]).then_inc(h2_done_s, 1)

            def layer3(t):
                act.wait_ge(y_summed, t + 1)
                nc.scalar.copy(y_sb[:, t * P:(t + 1) * P], y_ps).then_inc(y_copied, 1)

            for o in range(2):
                shift_ids(o)
                split_table(o)
            for step, *at in order:
                if step == "lookup":
                    copy_lookup(*at)
                    if at[0] + 2 < NO:
                        split_table(at[0] + 2)
                        shift_ids(at[0] + 2)
                elif step == "turn":
                    copy_turned(*at)
                elif step == "dots":
                    copy_dots(*at)
                elif step == "spread_left":
                    spread_left(*at)
                elif step == "fold":
                    copy_fold(*at)
                elif step == "layer1":
                    layer1(*at)
                elif step == "layer2":
                    layer2(*at)
                elif step == "layer3":
                    layer3(*at)

        @block.vector
        def _(dve):
            nc.vector.memset(emb_t[:, :, :, :, NF:SLOTS].rearrange("d t i j s -> d (t i j) s"), 0.0).then_inc(pads_zeroed, 1)

            def lower_part(o):
                dve.wait_ge(hi_made, o + 1)
                nc.vector.tensor_tensor(table_lo[0:TP, o % SPLIT, :, :], table[0:TP, o % RAW, :, :],
                                        table_hi[0:TP, o % SPLIT, :, :].bitcast(F32),
                                        ALU.subtract).then_inc(lo_made, 1)

            def make_onehot(o):
                dve.wait_ge(ids_shifted, o + 1)
                for c in range(CHUNKS):
                    n = o * CHUNKS + c
                    if n >= ONEHOT_CHUNKS:
                        dve.wait_ge(onehot_used, n - ONEHOT_CHUNKS + 1)
                    nc.vector.tensor_single_scalar(onehot[0:TP, n % ONEHOT_CHUNKS, :], ids_rel[0:TP, o % 2, :],
                                                   float(c), op=ALU.is_equal).then_inc(onehot_made, 1)

            def copy_dots(t, fill):
                n = t * FILLS + fill
                dve.wait_ge(dots_filled, n + 1)
                if t >= 1 and fill == 0:
                    dve.wait_ge(dots_turned, t)
                for j in (0, 1):
                    last = nc.vector.tensor_copy(dots_dst(j, fill), dots_src(j, n))
                last.then_inc(dots_copied_v, 1)

            def spread(t):
                dve.wait_ge(dots_copied_v, (t + 1) * FILLS)
                dve.wait_ge(dots_copied_s, (t + 1) * FILLS)
                if t >= 1:
                    dve.wait_ge(fold_left, t)
                    dve.wait_ge(fold_made, t)
                nc.vector.transpose(dots_t[:, :, :].rearrange("p g s -> p (g s)"),
                                    dots[:, :, :].rearrange("p g i -> p (g i)")).then_inc(dots_turned, 1)
                dve.wait_ge(dots_turned, t + 1)
                if t >= 1:
                    dve.wait_ge(fold_turned, t)
                nc.vector.tensor_copy(fold[:, :, 14:NF], dots_t[:, 14:NF, 14:NF]).then_inc(fold_base, 1)
                dve.wait_ge(fold_base, t + 1)
                nc.vector.copy_predicated(fold[:, :, 14:NF], fold_mask[:, :, :],
                                          dots_t[:, 0:ROWS, 1:1 + ROWS]).then_inc(fold_made, 1)

            def copy_fold(t):
                cols = slice(t * P, (t + 1) * P)
                dve.wait_ge(fold_turned, t + 1)
                nc.vector.tensor_copy(feat_t[:, 0:KT - 1, cols],
                                      fold_v_ps[:, 0:(KT - 1) * P].rearrange("p (k b) -> p k b", b=P)
                                      ).then_inc(feat_copied, 1)

            def layer1(t):
                if t == 0:
                    dve.wait_ge(weights_in, 16 * 7)
                else:
                    dve.wait_ge(y_summed, t)
                dve.wait_ge(h1_summed, 2 * t + 1)
                for i in range(M1 // 2):
                    n = 2 * i
                    nc.vector.tensor_scalar(h1[:, n, :], layer_ps[0][:, i * P:(i + 1) * P], b1_sb[:, n:n + 1], 0.0,
                                            ALU.add, ALU.max).then_inc(h1_done_v, 1)

            def layer2(t):
                dve.wait_ge(h2_summed, t * M2 + 1)
                nc.vector.tensor_scalar(h2[:, 0, :], layer_ps[0][:, 0:P], b2_sb[:, 0:1], 0.0,
                                        ALU.add, ALU.max).then_inc(h2_done_v, 1)

            for step, *at in order:
                if step == "lookup" and at[0] == 0:
                    make_onehot(0)
                    lower_part(0)
                elif step == "lookup":
                    lower_part(*at)
                    make_onehot(*at)
                elif step == "dots":
                    copy_dots(*at)
                elif step == "spread":
                    spread(*at)
                elif step == "fold":
                    copy_fold(*at)
                elif step == "layer1":
                    layer1(*at)
                elif step == "layer2":
                    layer2(*at)


def kernel(**inputs):
    import numpy as np
    import concourse.bacc as bacc
    from concourse.bass_utils import run_bass_kernel_spmd as run

    nc = bacc.Bacc("TRN2", target_bir_lowering=False, num_devices=1)
    arrays = {}

    def given(name, a):
        a = np.ascontiguousarray(a)
        arrays["in_" + name] = a
        return nc.dram_tensor("in_" + name, a.shape, mybir.dt.from_np(a.dtype), kind="ExternalInput").ap()

    ids = np.asarray(inputs["ids"])
    w1 = np.asarray(inputs["W_top1"])
    pair = []
    for a, b in fold_order():
        hi, lo = max(SLOT_FEATURE[a], SLOT_FEATURE[b]), min(SLOT_FEATURE[a], SLOT_FEATURE[b])
        pair.append(hi * (hi - 1) // 2 + lo)
    order = pair + list(range(PAIRS, w1.shape[0]))
    args = [
        given("ids_pt", ids.reshape(TILES, P, NF).transpose(1, 0, 2).reshape(P, TILES * NF)),
        given("ids_oh", ids.T[ONEHOT].reshape(NO * B)),
        [given(f"tbl_{f}", inputs[f"tbl_{f}"]) for f in range(NF)],
        given("dense_t", np.asarray(inputs["dense_ctx"]).T),
        given("w1", w1[order]),
        given("b1", np.asarray(inputs["b_top1"]).reshape(-1, P).T),
        given("w2", inputs["W_top2"]),
        given("b2", np.asarray(inputs["b_top2"]).reshape(-1, P).T),
        given("w3", np.asarray(inputs["W_top3"]).reshape(-1, P).T),
    ]
    out = nc.dram_tensor("out_y", (B, 1), F32, kind="ExternalOutput").ap()
    dlrm_tower(nc, *args, out)
    r = run(nc, [arrays], core_ids=[0])
    return r.results[0]["out_y"]
```

```python
from contextlib import ExitStack

import concourse.bass as bass
from concourse import mybir

F32 = mybir.dt.float32
F32R = mybir.dt.float32r
I32 = mybir.dt.int32
ALU = mybir.AluOpType
ACT = mybir.ActivationFunctionType

P = 128
NF = 27
D = 128
B = 512
TILES = B // P
SLOTS = 32
QUADS = P // 4
ROWS = NF // 2
PAIRS = ROWS * NF
ONEHOT_ROWS = 1000
CHUNKS = 8
TP = ONEHOT_ROWS // CHUNKS
TS = 120
ONEHOT = [0, 1, 2, 5, 8, 16, 18, 20, 21]
GATHERED = [f for f in range(NF) if f not in ONEHOT]
SLOT_FEATURE = GATHERED + ONEHOT
NG, NO = len(GATHERED), len(ONEHOT)
HALVED = 2
GROUPS = (NG + 3) // 4
QB = 4
IDS_PARTS = [range(0, 1), range(1, 2), range(2, 3), range(3, 4), range(4, NO)]
RAW = 4
ONEHOT_CHUNKS = 12
SPLIT = 2
WARM_START = 8
ROW_TILES = 3
FILLS = QUADS // (2 * QB)
BESIDE = [
    ["turn.1.2", "turn.1.3", "turn.1.4", "spread.0 lower.0"],
    ["turn.2.0 upper.0", "fold.0 turn.2.1", "layer1.0 more1.0 relu1.0 turn.2.2",
     "spread.1 turn.2.3 lower.1 layer2.0 turn.2.4 upper.1 fold.1 layer3.0"],
    ["", "layer1.1 more1.1 relu1.1", "turn.3.0",
     "spread.2 turn.3.1 lower.2 layer2.1 turn.3.2 upper.2 fold.2 layer3.1 turn.3.3 layer1.2 turn.3.4 more1.2 relu1.2"],
    ["", "", "", "spread.3 lower.3 upper.3 layer2.2 fold.3 layer3.2 layer1.3 more1.3 relu1.3 layer2.3 layer3.3"],
]


def step_order():
    first = [("turn", 0, g) for g in range(GROUPS)]
    order = []
    for o in range(NO):
        order.append(("lookup", o))
        if o >= NO - 1 - GROUPS and first:
            order.append(first.pop(0))
    order += first
    order += [("turn", 1, g) for g in range(2)]
    for t, beside in enumerate(BESIDE):
        for n, steps in enumerate(beside):
            order.append(("dots", t, n))
            for step in steps.split():
                name, *at = step.split(".")
                order.append((name, *(int(a) for a in at)))
    return order


def group_slots(g):
    return range(4 * g, min(4 * g + 4, NG))


def table_parts(o):
    return [slice(0, CHUNKS // 2), slice(CHUNKS // 2, CHUNKS)] if o < HALVED else [slice(0, CHUNKS)]


def fill_parts(n):
    return [slice(0, 1), slice(1, 2)] if n == TILES * FILLS - 1 else [slice(0, 2)]


def load_parts(o):
    return table_parts(o) if o == 0 else [slice(0, CHUNKS)]


def parts_through(o):
    return sum(len(table_parts(n)) for n in range(o + 1))


def fold_order():
    order = []
    for r in range(ROWS):
        for c in range(NF):
            order.append((14 + r, c) if c < 14 + r else (c - 13, r))
    return order


def dlrm_tower(nc, ids_pt, ids_oh, tables, dense_t, w1, b1, w2, b2, w3, out):
    N1, N2 = w1.shape[1], w2.shape[1]
    K1 = w1.shape[0]
    KT = (K1 + P - 1) // P
    KL = K1 - (KT - 1) * P
    ZL = PAIRS - (KT - 1) * P
    M1, M2 = N1 // P, N2 // P

    with ExitStack() as ctx:
        def sb(name, shape, dt=F32):
            return ctx.enter_context(nc.sbuf_tensor(name, shape, dt))

        def ps(name, shape):
            return ctx.enter_context(nc.psum_tensor(name, shape, F32))

        def sem(name):
            return ctx.enter_context(nc.semaphore(name))

        ident = sb("ident", [P, P])
        fold_mask = sb("fold_mask", [P, ROWS, ROWS], I32)
        first_row = sb("first_row", [P, 1])
        ids_sb = sb("ids_sb", [P, TILES * NF], I32)
        ids_row = sb("ids_row", [P, NO, B], I32)
        ids_rel = sb("ids_rel", [P, 2, B])
        rows = sb("rows", [P, ROW_TILES, NG, D])
        table = sb("table", [P, RAW, CHUNKS, D])
        table_hi = sb("table_hi", [P, SPLIT, CHUNKS, D], F32R)
        table_lo = sb("table_lo", [P, SPLIT, CHUNKS, D], F32R)
        onehot = sb("onehot", [P, ONEHOT_CHUNKS, B], F32R)
        emb_t = sb("emb_t", [P, TILES, QUADS, 4, SLOTS])
        dots = sb("dots", [P, NF, QUADS])
        dots_t = sb("dots_t", [P, NF, SLOTS])
        fold = sb("fold", [P, ROWS, NF])
        feat_t = sb("feat_t", [P, KT, B])
        w1_sb = sb("w1_sb", [P, KT, N1])
        w2_sb = sb("w2_sb", [P, M1, N2])
        w3_sb = sb("w3_sb", [P, M2])
        b1_sb = sb("b1_sb", [P, M1])
        b2_sb = sb("b2_sb", [P, M2])
        h1 = sb("h1", [P, M1, P])
        h2 = sb("h2", [P, M2, P])
        y_sb = sb("y_sb", [1, B])

        emb_ps = ps("emb_ps", [P, 2, 512])
        dots_ps = ps("dots_ps", [P, 2, 2, 512])
        layer_ps = [ps("layer_v_ps", [P, 512]), ps("layer_s_ps", [P, 512])]
        y_ps = layer_ps[0][0:1, 0:P]

        ids_in = sem("ids_in")
        ids_row_in = [sem(f"ids_row{n}_in") for n in range(len(IDS_PARTS))]
        table_in = [[sem(f"table{o}_{part}_in") for part in range(len(load_parts(o)))] for o in range(NO)]
        ids_shifted = sem("ids_shifted")
        weights_in = sem("weights_in")
        hi_made = sem("hi_made")
        lo_made = sem("lo_made")
        rows_in = [[sem(f"rows{t}_{g}_in") for g in range(GROUPS)] for t in range(TILES)]
        consts_set = sem("consts_set")
        consts_made = sem("consts_made")
        pads_zeroed = sem("pads_zeroed")
        onehot_made = sem("onehot_made")
        onehot_used = sem("onehot_used")
        lookup_copied = sem("lookup_copied")
        turned = sem("turned")
        turn_copied = sem("turn_copied")
        dots_filled = sem("dots_filled")
        dots_copied_v = sem("dots_copied_v")
        dots_copied_s = sem("dots_copied_s")
        dots_turned = sem("dots_turned")
        fold_base = sem("fold_base")
        fold_made = sem("fold_made")
        fold_copied = sem("fold_copied")
        last_fold_copied = sem("last_fold_copied")
        h1_summed = sem("h1_summed")
        h1_done_v = sem("h1_done_v")
        h1_done_s = sem("h1_done_s")
        h2_summed = sem("h2_summed")
        h2_done_v = sem("h2_done_v")
        h2_done_s = sem("h2_done_s")
        y_summed = sem("y_summed")
        y_copied = sem("y_copied")
        y_out = sem("y_out")

        order = step_order()
        emb_steps = [s for s in order if s[0] in ("turn", "fold")]
        emb_use = {step: n for n, step in enumerate(emb_steps)}

        def lookup_ps(o):
            return dots_ps[:, o // 2 % 2, o % 2, :]

        def fold_ps(t, k):
            n = emb_use["fold", t]
            if t == TILES - 1 and k == KT - 1:
                return emb_ps[:, (n + 1) % 2, 0:P]
            return emb_ps[:, n % 2, k * P:(k + 1) * P]

        def fold_ps_full(t):
            return emb_ps[:, emb_use["fold", t] % 2, 0:(KT - 1) * P].rearrange("p (k b) -> p k b", b=P)

        def h1_ps(t, n):
            if t == TILES - 1:
                return dots_ps[:, n // 2, n % 2, 0:P]
            return layer_ps[n % 2][:, n // 2 * P:(n // 2 + 1) * P]

        def h1_order(t):
            return list(range(M1)) if t == TILES - 1 else [*range(0, M1, 2), *range(1, M1, 2)]

        def h1_ready(t, n):
            own = h1_order(t).index(n if t == TILES - 1 else M1 - 2 + n % 2)
            return t * M1 + own + 1

        def dots_src(j, n, banks):
            return (dots_ps[32 * j:32 * j + 32, n % 2, banks, 0:QB * 4 * NF]
                    .rearrange("p k (q j g) -> p k q j g", q=QB, j=4)[:, :, :, j, :])

        def dots_dst(j, fill, banks):
            quads = slice((fill * 2 + banks.start) * QB, (fill * 2 + banks.stop) * QB)
            return dots[32 * j:32 * j + 32, :, quads].rearrange("p g (k q) -> p k q g", q=QB)

        block = ctx.enter_context(nc.Block())

        def load_table(sp, o):
            src = tables[ONEHOT[o]].rearrange("(p c) d -> p c d", c=CHUNKS)
            for part, chunks in enumerate(load_parts(o)):
                arrived = table_in[o][part]
                sp.dma_start(table[0:TS, o % RAW, chunks, :], src[0:TS, chunks]).then_inc(arrived, 16)
                sp.dma_start(table[TS:TP, o % RAW, chunks, :], src[TS:TP, chunks]).then_inc(arrived, 16)

        def load_ids(sp, n):
            part = IDS_PARTS[n]
            sp.dma_start(ids_row[:, part.start:part.stop, :].rearrange("p o b -> p (o b)"),
                         ids_oh[part.start * B:part.stop * B].partition_broadcast(P)).then_inc(ids_row_in[n], 16)

        def load_weights(sp):
            sp.dma_start(w1_sb[:, 0:KT - 1, :],
                         w1[0:(KT - 1) * P, :].rearrange("(k p) n -> p k n", p=P)).then_inc(weights_in, 16)
            sp.dma_start(w1_sb[0:KL, KT - 1, :], w1[(KT - 1) * P:K1, :]).then_inc(weights_in, 16)
            sp.dma_start(w2_sb[:, :, :], w2.rearrange("(k p) n -> p k n", p=P)).then_inc(weights_in, 16)
            sp.dma_start(feat_t[ZL:KL, KT - 1, :], dense_t).then_inc(weights_in, 16)
            sp.dma_start(w3_sb[:, :], w3).then_inc(weights_in, 16)
            sp.dma_start(b1_sb[:, :], b1).then_inc(weights_in, 16)
            sp.dma_start(b2_sb[:, :], b2).then_inc(weights_in, 16)

        @block.sync
        def _(sp):
            sp.dma_start(ids_sb[:, :], ids_pt).then_inc(ids_in, 16)
            load_ids(sp, 0)
            load_table(sp, 0)
            load_ids(sp, 1)
            load_table(sp, 1)
            load_ids(sp, 2)
            load_table(sp, 2)
            load_ids(sp, 3)
            load_table(sp, 3)
            load_ids(sp, 4)
            for o in range(RAW, NO):
                sp.wait_ge(lo_made, parts_through(o - RAW))
                load_table(sp, o)
                if o == RAW + 1:
                    load_weights(sp)
            sp.wait_ge(y_copied, TILES)
            sp.dma_start(out.rearrange("b o -> o b"), y_sb[:, :]).then_inc(y_out, 16)
            sp.wait_ge(y_out, 16)

        @block.gpsimd
        def _(pool):
            nc.gpsimd.memset(ident[:, :], 0.0).then_inc(consts_set, 1)
            nc.gpsimd.memset(fold_mask[:, :, :], 1).then_inc(consts_set, 1)
            nc.gpsimd.iota(first_row[:, :], [[0, 1]], base=0, channel_multiplier=-CHUNKS,
                           allow_small_or_imprecise_dtypes=True).then_inc(consts_made, 1)
            pool.wait_ge(consts_set, 2)
            nc.gpsimd.affine_select(out=ident[:, :], in_=ident[:, :], compare_op=ALU.not_equal, fill=1.0,
                                    base=0, pattern=[[-1, P]], channel_multiplier=1).then_inc(consts_made, 1)
            nc.gpsimd.affine_select(out=fold_mask[:, :, :], in_=fold_mask[:, :, :], compare_op=ALU.is_ge, fill=0.0,
                                    base=0, pattern=[[-1, ROWS], [1, ROWS]],
                                    channel_multiplier=0).then_inc(consts_made, 1)
            pool.wait_ge(ids_in, 16)
            for t in range(TILES):
                if t >= ROW_TILES:
                    pool.wait_ge(turned, emb_use["turn", t - ROW_TILES, GROUPS - 1] + 1)
                for g in range(GROUPS):
                    for slot in group_slots(g):
                        at = t * NF + SLOT_FEATURE[slot]
                        nc.gpsimd.indirect_dma_start(
                            rows[:, t % ROW_TILES, slot, :], None, tables[SLOT_FEATURE[slot]],
                            bass.IndirectOffsetOnAxis(ap=ids_sb[:, at:at + 1], axis=0)).then_inc(rows_in[t][g], 16)

        @block.tensor
        def _(pe):
            def warm_up(count):
                for _ in range(count):
                    nc.tensor.matmul(layer_ps[1][:, 0:P], ident[:, :], ident[:, :], start=True, stop=True)

            def lookup(o):
                if o >= 4:
                    pe.wait_ge(lookup_copied, o - 3)
                bank = lookup_ps(o)
                steps = [(part, c) for c in range(CHUNKS) for part in (table_hi, table_lo)]
                if o < HALVED:
                    steps = [(part, c) for half in table_parts(o) for part in (table_hi, table_lo)
                             for c in range(half.start, half.stop)]
                for n, (part, c) in enumerate(steps):
                    for i, chunks in enumerate(table_parts(o)):
                        if c == chunks.start:
                            pe.wait_ge(hi_made if part is table_hi else lo_made, parts_through(o - 1) + i + 1)
                    if part is table_hi:
                        pe.wait_ge(onehot_made, o * CHUNKS + c + 1)
                    mm = nc.tensor.matmul(bank, part[0:TP, o % SPLIT, c, :],
                                          onehot[0:TP, (o * CHUNKS + c) % ONEHOT_CHUNKS, :],
                                          start=(n == 0), stop=(n == len(steps) - 1))
                    if part is table_lo:
                        mm.then_inc(onehot_used, 1)

            def wait_copied(n):
                name, t = emb_steps[n][0:2]
                if name == "fold":
                    pe.wait_ge(fold_copied, t + 1)
                else:
                    pe.wait_ge(turn_copied, sum(s[0] == "turn" for s in emb_steps[0:n + 1]))

            def turn(t, g):
                n = emb_use["turn", t, g]
                if n >= 2:
                    wait_copied(n - 2)
                bank = emb_ps[:, n % 2, :]
                pe.wait_ge(rows_in[t][g], 16 * len(group_slots(g)))
                for i, slot in enumerate(group_slots(g)):
                    mm = nc.tensor.transpose(bank[:, i * P:(i + 1) * P],
                                             rows[:, t % ROW_TILES, slot, :], ident[:, :])
                mm.then_inc(turned, 1)

            def dots_fill(t, fill):
                n = t * FILLS + fill
                if fill == 0:
                    pe.wait_ge(lookup_copied, NO)
                    wait_copied(emb_use["turn", t, GROUPS - 1])
                if n >= 2:
                    pe.wait_ge(dots_copied_v, n - 1)
                    pe.wait_ge(dots_copied_s, n - 1)
                ends = [banks.stop * QB - 1 for banks in fill_parts(n)]
                for q in range(2 * QB):
                    i = fill * 2 * QB + q
                    at = (q % QB) * 4 * NF
                    mm = nc.tensor.matmul(dots_ps[:, n % 2, q // QB, at:at + 4 * NF],
                                          emb_t[:, t, i, :, :].rearrange("d j s -> d (j s)"),
                                          emb_t[:, t, i, :, 0:NF],
                                          start=True, stop=True)
                    if q in ends:
                        mm.then_inc(dots_filled, 1)

            def turn_fold(t):
                pairs = fold[:, :, :].rearrange("p r c -> p (r c)")
                pe.wait_ge(fold_made, t + 1)
                n = emb_use["fold", t]
                wait_copied(n - 2)
                if t == TILES - 1:
                    wait_copied(n - 1)
                for k in range(KT):
                    m = min(P, PAIRS - k * P)
                    mm = nc.tensor.transpose(fold_ps(t, k)[0:m, :], pairs[:, k * P:k * P + m], ident[:, :])
                mm.then_inc(turned, 1)

            def layer1(t, half):
                if t == 0:
                    pe.wait_ge(weights_in, 16 * 7)
                if t < TILES - 1:
                    pe.wait_ge(fold_copied, t + 1)
                else:
                    pe.wait_ge(last_fold_copied, 1)
                if 1 <= t < TILES - 1:
                    pe.wait_ge(h2_done_s, t)
                    pe.wait_ge(y_copied, t)
                ks = [KT - 1, *range(KT - 1)]
                for n in h1_order(t)[half * M1 // 2:(half + 1) * M1 // 2]:
                    for k in ks:
                        if t == TILES - 1 and n == 0 and k < KT - 1:
                            pe.wait_ge(fold_copied, t + k + 1)
                        rows_k = P if k < KT - 1 else KL
                        mm = nc.tensor.matmul(h1_ps(t, n), w1_sb[0:rows_k, k, n * P:(n + 1) * P],
                                              feat_t[0:rows_k, k, t * P:(t + 1) * P],
                                              start=(k == ks[0]), stop=(k == ks[-1]))
                    mm.then_inc(h1_summed, 1)

            def layer2(t):
                if t == TILES - 1:
                    pe.wait_ge(y_copied, t)
                ks = h1_order(t)
                for n in range(M2):
                    for k in ks:
                        if n == 0:
                            done = t * M1 // 2 + (k // 2 + 1 if t == TILES - 1 else M1 // 2)
                            pe.wait_ge((h1_done_v, h1_done_s)[k % 2], done)
                        mm = nc.tensor.matmul(layer_ps[n][:, 0:P], w2_sb[:, k, n * P:(n + 1) * P],
                                              h1[:, k, :], start=(k == ks[0]), stop=(k == ks[-1]))
                    mm.then_inc(h2_summed, 1)

            def layer3(t):
                for k in range(M2):
                    pe.wait_ge((h2_done_v, h2_done_s)[k], t + 1)
                    mm = nc.tensor.matmul(y_ps, w3_sb[:, k:k + 1], h2[:, k, :],
                                          start=(k == 0), stop=(k == M2 - 1))
                mm.then_inc(y_summed, 1)

            pe.wait_ge(consts_made, 3)
            warm_up(WARM_START)
            for step, *at in order:
                if step == "lookup":
                    lookup(*at)
                elif step == "turn":
                    turn(*at)
                elif step == "dots":
                    dots_fill(*at)
                elif step == "fold":
                    turn_fold(*at)
                elif step == "layer1":
                    layer1(*at, 0)
                elif step == "more1":
                    layer1(*at, 1)
                elif step == "layer2":
                    layer2(*at)
                elif step == "layer3":
                    layer3(*at)

        @block.scalar
        def _(act):
            def split_table(o):
                if o >= SPLIT:
                    act.wait_ge(onehot_used, (o - SPLIT + 1) * CHUNKS)
                for part, chunks in enumerate(table_parts(o)):
                    act.wait_ge(table_in[o][min(part, len(load_parts(o)) - 1)], 32)
                    nc.scalar.copy(table_hi[0:TP, o % SPLIT, chunks, :],
                                   table[0:TP, o % RAW, chunks, :]).then_inc(hi_made, 1)

            def shift_ids(o):
                act.wait_ge(ids_row_in[[o in part for part in IDS_PARTS].index(True)], 16)
                if o == 0:
                    act.wait_ge(consts_made, 3)
                if o >= 2:
                    act.wait_ge(onehot_made, (o - 1) * CHUNKS)
                nc.scalar.activation(ids_rel[0:TP, o % 2, :], ids_row[0:TP, o, :], ACT.Identity,
                                     bias=first_row[0:TP, :]).then_inc(ids_shifted, 1)

            def copy_lookup(o):
                act.wait_ge(onehot_used, (o + 1) * CHUNKS)
                if o == 0:
                    act.wait_ge(pads_zeroed, 1)
                nc.scalar.copy(emb_t[:, :, :, :, NG + o].rearrange("d t i j -> d t j i"),
                               lookup_ps(o).rearrange("d (t j i) -> d t j i", j=4, i=QUADS)
                               ).then_inc(lookup_copied, 1)

            def copy_turned(t, g):
                use, n = emb_use["turn", t, g], len(group_slots(g))
                act.wait_ge(turned, use + 1)
                nc.scalar.copy(emb_t[:, t, :, :, 4 * g:4 * g + n].rearrange("d i j s -> d s j i"),
                               emb_ps[:, use % 2, 0:n * P].rearrange("d (s j i) -> d s j i", s=n, j=4)
                               ).then_inc(turn_copied, 1)

            def copy_dots(t, fill):
                n = t * FILLS + fill
                if t >= 1 and fill == 0:
                    act.wait_ge(dots_turned, 2 * t)
                for part, banks in enumerate(fill_parts(n)):
                    act.wait_ge(dots_filled, n + 1 + part)
                    for j in (2, 3):
                        last = nc.scalar.copy(dots_dst(j, fill, banks), dots_src(j, n, banks))
                last.then_inc(dots_copied_s, 1)

            def lower(t):
                act.wait_ge(dots_turned, 2 * t + 1)
                if t >= 1:
                    act.wait_ge(turned, emb_use["fold", t - 1] + 1)
                nc.scalar.copy(fold[:, :, :], dots_t[:, NF - ROWS:NF, 0:NF]).then_inc(fold_base, 1)

            def copy_last_fold(t):
                act.wait_ge(turned, emb_use["fold", t] + 1)
                nc.scalar.copy(feat_t[0:ZL, KT - 1, t * P:(t + 1) * P],
                               fold_ps(t, KT - 1)[0:ZL, :]).then_inc(last_fold_copied, 1)

            def layer1(t):
                if t == 0:
                    act.wait_ge(weights_in, 16 * 7)
                else:
                    act.wait_ge(y_summed, t)
                for n in range(1, M1, 2):
                    act.wait_ge(h1_summed, h1_ready(t, n))
                    nc.scalar.activation(h1[:, n, :], h1_ps(t, n), ACT.Relu,
                                         bias=b1_sb[:, n:n + 1]).then_inc(h1_done_s, 1)

            def layer2(t):
                act.wait_ge(h2_summed, t * M2 + 2)
                nc.scalar.activation(h2[:, 1, :], layer_ps[1][:, 0:P], ACT.Relu,
                                     bias=b2_sb[:, 1:2]).then_inc(h2_done_s, 1)

            def layer3(t):
                act.wait_ge(y_summed, t + 1)
                nc.scalar.copy(y_sb[:, t * P:(t + 1) * P], y_ps).then_inc(y_copied, 1)

            for o in range(2):
                shift_ids(o)
                split_table(o)
            for step, *at in order:
                if step == "lookup":
                    copy_lookup(*at)
                    if at[0] + 2 < NO:
                        split_table(at[0] + 2)
                        shift_ids(at[0] + 2)
                elif step == "turn":
                    copy_turned(*at)
                elif step == "dots":
                    copy_dots(*at)
                elif step == "lower":
                    lower(*at)
                elif step == "fold" and at[0] == TILES - 1:
                    copy_last_fold(*at)
                elif step == "relu1":
                    layer1(*at)
                elif step == "layer2":
                    layer2(*at)
                elif step == "layer3":
                    layer3(*at)

        @block.vector
        def _(dve):
            nc.vector.memset(emb_t[:, :, :, :, NF:SLOTS].rearrange("d t i j s -> d (t i j) s"), 0.0).then_inc(pads_zeroed, 1)

            def lower_part(o, part):
                chunks = table_parts(o)[part]
                dve.wait_ge(hi_made, parts_through(o - 1) + part + 1)
                nc.vector.tensor_tensor(table_lo[0:TP, o % SPLIT, chunks, :], table[0:TP, o % RAW, chunks, :],
                                        table_hi[0:TP, o % SPLIT, chunks, :].bitcast(F32),
                                        ALU.subtract).then_inc(lo_made, 1)

            def make_onehot(o, chunks):
                at_once = o == 0 and chunks.start == 0
                if at_once:
                    dve.wait_ge(ids_row_in[0], 16)
                    dve.wait_ge(consts_made, 3)
                else:
                    dve.wait_ge(ids_shifted, o + 1)
                for c in range(chunks.start, chunks.stop):
                    n = o * CHUNKS + c
                    if n >= ONEHOT_CHUNKS:
                        dve.wait_ge(onehot_used, n - ONEHOT_CHUNKS + 1)
                    to = onehot[0:TP, n % ONEHOT_CHUNKS, :]
                    if at_once:
                        nc.vector.tensor_scalar(to, ids_row[0:TP, o, :], first_row[0:TP, :], float(c),
                                                ALU.add, ALU.is_equal).then_inc(onehot_made, 1)
                    else:
                        nc.vector.tensor_single_scalar(to, ids_rel[0:TP, o % 2, :], float(c),
                                                       op=ALU.is_equal).then_inc(onehot_made, 1)

            def copy_dots(t, fill):
                n = t * FILLS + fill
                if t >= 1 and fill == 0:
                    dve.wait_ge(dots_turned, 2 * t)
                for part, banks in enumerate(fill_parts(n)):
                    dve.wait_ge(dots_filled, n + 1 + part)
                    for j in (0, 1):
                        last = nc.vector.tensor_copy(dots_dst(j, fill, banks), dots_src(j, n, banks))
                last.then_inc(dots_copied_v, 1)

            def spread(t):
                dve.wait_ge(dots_copied_v, (t + 1) * FILLS)
                dve.wait_ge(dots_copied_s, (t + 1) * FILLS)
                if t >= 1:
                    dve.wait_ge(fold_base, t)
                    dve.wait_ge(fold_made, t)
                for rows_of in (slice(NF - ROWS, NF), slice(0, ROWS)):
                    nc.vector.transpose(dots_t[:, rows_of, :].rearrange("p g s -> p (g s)"),
                                        dots[:, rows_of, :].rearrange("p g i -> p (g i)")
                                        ).then_inc(dots_turned, 1)

            def upper(t):
                dve.wait_ge(dots_turned, 2 * t + 2)
                dve.wait_ge(fold_base, t + 1)
                nc.vector.copy_predicated(fold[:, :, 14:NF], fold_mask[:, :, :],
                                          dots_t[:, 0:ROWS, 1:1 + ROWS]).then_inc(fold_made, 1)

            def copy_fold(t):
                cols = slice(t * P, (t + 1) * P)
                dve.wait_ge(turned, emb_use["fold", t] + 1)
                if t < TILES - 1:
                    nc.vector.tensor_copy(feat_t[:, 0:KT - 1, cols], fold_ps_full(t))
                    nc.vector.tensor_copy(feat_t[0:ZL, KT - 1, cols],
                                          fold_ps(t, KT - 1)[0:ZL, :]).then_inc(fold_copied, 1)
                else:
                    for k in range(KT - 1):
                        nc.vector.tensor_copy(feat_t[:, k, cols], fold_ps(t, k)).then_inc(fold_copied, 1)

            def layer1(t):
                if t == 0:
                    dve.wait_ge(weights_in, 16 * 7)
                else:
                    dve.wait_ge(y_summed, t)
                for n in range(0, M1, 2):
                    dve.wait_ge(h1_summed, h1_ready(t, n))
                    nc.vector.tensor_scalar(h1[:, n, :], h1_ps(t, n), b1_sb[:, n:n + 1], 0.0,
                                            ALU.add, ALU.max).then_inc(h1_done_v, 1)

            def layer2(t):
                dve.wait_ge(h2_summed, t * M2 + 1)
                nc.vector.tensor_scalar(h2[:, 0, :], layer_ps[0][:, 0:P], b2_sb[:, 0:1], 0.0,
                                        ALU.add, ALU.max).then_inc(h2_done_v, 1)

            for step, *at in order:
                if step == "lookup":
                    o = at[0]
                    for part, chunks in enumerate(table_parts(o)):
                        if o < HALVED:
                            make_onehot(o, chunks)
                            lower_part(o, part)
                        else:
                            lower_part(o, part)
                            make_onehot(o, chunks)
                elif step == "dots":
                    copy_dots(*at)
                elif step == "spread":
                    spread(*at)
                elif step == "upper":
                    upper(*at)
                elif step == "fold":
                    copy_fold(*at)
                elif step == "layer1":
                    layer1(*at)
                elif step == "layer2":
                    layer2(*at)


def kernel(**inputs):
    import numpy as np
    import concourse.bacc as bacc
    from concourse.bass_utils import run_bass_kernel_spmd as run

    nc = bacc.Bacc("TRN2", target_bir_lowering=False, num_devices=1)
    arrays = {}

    def given(name, a):
        a = np.ascontiguousarray(a)
        arrays["in_" + name] = a
        return nc.dram_tensor("in_" + name, a.shape, mybir.dt.from_np(a.dtype), kind="ExternalInput").ap()

    ids = np.asarray(inputs["ids"])
    w1 = np.asarray(inputs["W_top1"])
    pair = []
    for a, b in fold_order():
        hi, lo = max(SLOT_FEATURE[a], SLOT_FEATURE[b]), min(SLOT_FEATURE[a], SLOT_FEATURE[b])
        pair.append(hi * (hi - 1) // 2 + lo)
    order = pair + list(range(PAIRS, w1.shape[0]))
    args = [
        given("ids_pt", ids.reshape(TILES, P, NF).transpose(1, 0, 2).reshape(P, TILES * NF)),
        given("ids_oh", ids.T[ONEHOT].reshape(NO * B)),
        [given(f"tbl_{f}", inputs[f"tbl_{f}"]) for f in range(NF)],
        given("dense_t", np.asarray(inputs["dense_ctx"]).T),
        given("w1", w1[order]),
        given("b1", np.asarray(inputs["b_top1"]).reshape(-1, P).T),
        given("w2", inputs["W_top2"]),
        given("b2", np.asarray(inputs["b_top2"]).reshape(-1, P).T),
        given("w3", np.asarray(inputs["W_top3"]).reshape(-1, P).T),
    ]
    out = nc.dram_tensor("out_y", (B, 1), F32, kind="ExternalOutput").ap()
    dlrm_tower(nc, *args, out)
    r = run(nc, [arrays], core_ids=[0])
    return r.results[0]["out_y"]
```
